# Optimizing a Trainium2 kernel written in Bass

```python
import numpy as np
import jax
import jax.numpy as jnp

def _softmax(x, axis=-1):
    return jax.nn.softmax(x, axis=axis)

def _gelu(x):
    return jax.nn.gelu(x, approximate=True)

def _silu(x):
    return jax.nn.silu(x)

def _sigmoid(x):
    return jax.nn.sigmoid(x)

def _layernorm(x, axis=-1, eps=1e-05):
    m = jnp.mean(x, axis=axis, keepdims=True)
    v = jnp.var(x, axis=axis, keepdims=True)
    return (x - m) / jnp.sqrt(v + eps)

def _scatter_add(tgt, idx, src, axis=0):
    return tgt.at[idx].add(src)

def _segment_sum(src, seg, n):
    return jax.ops.segment_sum(src, seg, n)
kernel_name = 'mk_dlrm_tower_d1_rec_r8_495121'

def setup_inputs(seed: int=0):
    np.random.seed(seed)
    _w = jnp.asarray

    def _rec_inputs():
        import jax
        import jax.numpy as jnp
        _tk = jax.random.key(seed)
        dense_ctx = jax.random.normal(jax.random.fold_in(_tk, 190), (512, 16), jnp.float32)
        ids = jnp.stack([jax.random.randint(jax.random.fold_in(_tk, 200 + f), (512,), 0, v, jnp.int32) for f, v in enumerate([12500, 1000, 12500, 1250, 1000, 125000, 1000, 12500, 125000, 12500, 1000, 12500, 1000, 1250, 1000, 1250, 1250, 1250, 1000, 12500, 125000, 1000, 1250, 12500, 12500, 125000, 125000, 1000, 125000, 12500, 12500, 12500])], axis=1)
        tbl_0 = 0.05 * jax.random.normal(jax.random.fold_in(_tk, 500 + 0), (12500, 16), jnp.float32)
        tbl_1 = 0.05 * jax.random.normal(jax.random.fold_in(_tk, 500 + 1), (1000, 16), jnp.float32)
        tbl_2 = 0.05 * jax.random.normal(jax.random.fold_in(_tk, 500 + 2), (12500, 16), jnp.float32)
        tbl_3 = 0.05 * jax.random.normal(jax.random.fold_in(_tk, 500 + 3), (1250, 16), jnp.float32)
        tbl_4 = 0.05 * jax.random.normal(jax.random.fold_in(_tk, 500 + 4), (1000, 16), jnp.float32)
        tbl_5 = 0.05 * jax.random.normal(jax.random.fold_in(_tk, 500 + 5), (125000, 16), jnp.float32)
        tbl_6 = 0.05 * jax.random.normal(jax.random.fold_in(_tk, 500 + 6), (1000, 16), jnp.float32)
        tbl_7 = 0.05 * jax.random.normal(jax.random.fold_in(_tk, 500 + 7), (12500, 16), jnp.float32)
        tbl_8 = 0.05 * jax.random.normal(jax.random.fold_in(_tk, 500 + 8), (125000, 16), jnp.float32)
        tbl_9 = 0.05 * jax.random.normal(jax.random.fold_in(_tk, 500 + 9), (12500, 16), jnp.float32)
        tbl_10 = 0.05 * jax.random.normal(jax.random.fold_in(_tk, 500 + 10), (1000, 16), jnp.float32)
        tbl_11 = 0.05 * jax.random.normal(jax.random.fold_in(_tk, 500 + 11), (12500, 16), jnp.float32)
        tbl_12 = 0.05 * jax.random.normal(jax.random.fold_in(_tk, 500 + 12), (1000, 16), jnp.float32)
        tbl_13 = 0.05 * jax.random.normal(jax.random.fold_in(_tk, 500 + 13), (1250, 16), jnp.float32)
        tbl_14 = 0.05 * jax.random.normal(jax.random.fold_in(_tk, 500 + 14), (1000, 16), jnp.float32)
        tbl_15 = 0.05 * jax.random.normal(jax.random.fold_in(_tk, 500 + 15), (1250, 16), jnp.float32)
        tbl_16 = 0.05 * jax.random.normal(jax.random.fold_in(_tk, 500 + 16), (1250, 16), jnp.float32)
        tbl_17 = 0.05 * jax.random.normal(jax.random.fold_in(_tk, 500 + 17), (1250, 16), jnp.float32)
        tbl_18 = 0.05 * jax.random.normal(jax.random.fold_in(_tk, 500 + 18), (1000, 16), jnp.float32)
        tbl_19 = 0.05 * jax.random.normal(jax.random.fold_in(_tk, 500 + 19), (12500, 16), jnp.float32)
        tbl_20 = 0.05 * jax.random.normal(jax.random.fold_in(_tk, 500 + 20), (125000, 16), jnp.float32)
        tbl_21 = 0.05 * jax.random.normal(jax.random.fold_in(_tk, 500 + 21), (1000, 16), jnp.float32)
        tbl_22 = 0.05 * jax.random.normal(jax.random.fold_in(_tk, 500 + 22), (1250, 16), jnp.float32)
        tbl_23 = 0.05 * jax.random.normal(jax.random.fold_in(_tk, 500 + 23), (12500, 16), jnp.float32)
        tbl_24 = 0.05 * jax.random.normal(jax.random.fold_in(_tk, 500 + 24), (12500, 16), jnp.float32)
        tbl_25 = 0.05 * jax.random.normal(jax.random.fold_in(_tk, 500 + 25), (125000, 16), jnp.float32)
        tbl_26 = 0.05 * jax.random.normal(jax.random.fold_in(_tk, 500 + 26), (125000, 16), jnp.float32)
        tbl_27 = 0.05 * jax.random.normal(jax.random.fold_in(_tk, 500 + 27), (1000, 16), jnp.float32)
        tbl_28 = 0.05 * jax.random.normal(jax.random.fold_in(_tk, 500 + 28), (125000, 16), jnp.float32)
        tbl_29 = 0.05 * jax.random.normal(jax.random.fold_in(_tk, 500 + 29), (12500, 16), jnp.float32)
        tbl_30 = 0.05 * jax.random.normal(jax.random.fold_in(_tk, 500 + 30), (12500, 16), jnp.float32)
        tbl_31 = 0.05 * jax.random.normal(jax.random.fold_in(_tk, 500 + 31), (12500, 16), jnp.float32)
        _rk = jax.random.fold_in(_tk, 7)
        W_top1 = 0.0606339 * jax.random.normal(jax.random.fold_in(_tk, 801), (272, 512), jnp.float32)
        W_top2 = 0.0441942 * jax.random.normal(jax.random.fold_in(_tk, 802), (512, 256), jnp.float32)
        W_top3 = 0.0625 * jax.random.normal(jax.random.fold_in(_tk, 803), (256, 1), jnp.float32)
        b_top1 = jnp.zeros((512,), jnp.float32)
        b_top2 = jnp.zeros((256,), jnp.float32)
        return (dense_ctx, ids, tbl_0, tbl_1, tbl_2, tbl_3, tbl_4, tbl_5, tbl_6, tbl_7, tbl_8, tbl_9, tbl_10, tbl_11, tbl_12, tbl_13, tbl_14, tbl_15, tbl_16, tbl_17, tbl_18, tbl_19, tbl_20, tbl_21, tbl_22, tbl_23, tbl_24, tbl_25, tbl_26, tbl_27, tbl_28, tbl_29, tbl_30, tbl_31, W_top1, b_top1, W_top2, b_top2, W_top3)
    dense_ctx, ids, tbl_0, tbl_1, tbl_2, tbl_3, tbl_4, tbl_5, tbl_6, tbl_7, tbl_8, tbl_9, tbl_10, tbl_11, tbl_12, tbl_13, tbl_14, tbl_15, tbl_16, tbl_17, tbl_18, tbl_19, tbl_20, tbl_21, tbl_22, tbl_23, tbl_24, tbl_25, tbl_26, tbl_27, tbl_28, tbl_29, tbl_30, tbl_31, W_top1, b_top1, W_top2, b_top2, W_top3 = _rec_inputs()

    def _L0_rec_setup():
        import jax, jax.numpy as jnp
        import numpy as np
        NUM_FIELDS = 32
        EMBED_DIM = 16
        BATCH = 512
        CROSS_SIZES = [128, 128, 128]

        def _cin_forward(x, Ws, bs):
            x0 = x
            h = x
            xs = []
            n_layers = len(Ws)
            for i in range(n_layers):
                B, F, E = x0.shape
                G = h.shape[1]
                z = (x0[:, :, None, :] * h[:, None, :, :]).reshape(B, F * G, E)
                y = jax.nn.relu(jnp.einsum('oc,bce->boe', Ws[i], z) + bs[i][None, :, None])
                if i != n_layers - 1:
                    half = y.shape[1] // 2
                    x_keep, h = (y[:, :half, :], y[:, half:, :])
                else:
                    x_keep, h = (y, y)
                xs.append(x_keep)
            return jnp.sum(jnp.concatenate(xs, axis=1), axis=2)
        key = jax.random.key(seed)
        ks = jax.random.split(key, 8)
        x = jax.random.normal(ks[0], (BATCH, NUM_FIELDS, EMBED_DIM), dtype=jnp.float32)
        prev = NUM_FIELDS
        inp = {'x': x}
        for i, cs in enumerate(CROSS_SIZES):
            in_ch = NUM_FIELDS * prev
            scale = 1.0 / np.sqrt(in_ch)
            inp[f'W{i}'] = jax.random.uniform(ks[1 + 2 * i], (cs, in_ch), dtype=jnp.float32, minval=-scale, maxval=scale)
            inp[f'b{i}'] = jax.random.uniform(ks[2 + 2 * i], (cs,), dtype=jnp.float32, minval=-scale, maxval=scale)
            prev = cs // 2
        return inp
    _L0_rec_all = _L0_rec_setup()
    _L0_rec_in = {k: v for k, v in _L0_rec_all.items() if k in ('W0', 'b0', 'W1', 'b1', 'W2', 'b2')}
    del _L0_rec_all
    return {'dense_ctx': dense_ctx, 'ids': ids, 'tbl_0': tbl_0, 'tbl_1': tbl_1, 'tbl_2': tbl_2, 'tbl_3': tbl_3, 'tbl_4': tbl_4, 'tbl_5': tbl_5, 'tbl_6': tbl_6, 'tbl_7': tbl_7, 'tbl_8': tbl_8, 'tbl_9': tbl_9, 'tbl_10': tbl_10, 'tbl_11': tbl_11, 'tbl_12': tbl_12, 'tbl_13': tbl_13, 'tbl_14': tbl_14, 'tbl_15': tbl_15, 'tbl_16': tbl_16, 'tbl_17': tbl_17, 'tbl_18': tbl_18, 'tbl_19': tbl_19, 'tbl_20': tbl_20, 'tbl_21': tbl_21, 'tbl_22': tbl_22, 'tbl_23': tbl_23, 'tbl_24': tbl_24, 'tbl_25': tbl_25, 'tbl_26': tbl_26, 'tbl_27': tbl_27, 'tbl_28': tbl_28, 'tbl_29': tbl_29, 'tbl_30': tbl_30, 'tbl_31': tbl_31, 'W_top1': W_top1, 'b_top1': b_top1, 'W_top2': W_top2, 'b_top2': b_top2, 'W_top3': W_top3, 'L0_rec_W0': _L0_rec_in['W0'], 'L0_rec_b0': _L0_rec_in['b0'], 'L0_rec_W1': _L0_rec_in['W1'], 'L0_rec_b1': _L0_rec_in['b1'], 'L0_rec_W2': _L0_rec_in['W2'], 'L0_rec_b2': _L0_rec_in['b2']}

def reference(dense_ctx, ids, tbl_0, tbl_1, tbl_2, tbl_3, tbl_4, tbl_5, tbl_6, tbl_7, tbl_8, tbl_9, tbl_10, tbl_11, tbl_12, tbl_13, tbl_14, tbl_15, tbl_16, tbl_17, tbl_18, tbl_19, tbl_20, tbl_21, tbl_22, tbl_23, tbl_24, tbl_25, tbl_26, tbl_27, tbl_28, tbl_29, tbl_30, tbl_31, W_top1, b_top1, W_top2, b_top2, W_top3, L0_rec_W0, L0_rec_b0, L0_rec_W1, L0_rec_b1, L0_rec_W2, L0_rec_b2):
    import jax
    import jax.numpy as jnp

    def _L0_rec_ref(x, W0, b0, W1, b1, W2, b2):
        import jax, jax.numpy as jnp
        import numpy as np
        NUM_FIELDS = 32
        EMBED_DIM = 16
        BATCH = 512
        CROSS_SIZES = [128, 128, 128]

        def _cin_forward(x, Ws, bs):
            x0 = x
            h = x
            xs = []
            n_layers = len(Ws)
            for i in range(n_layers):
                B, F, E = x0.shape
                G = h.shape[1]
                z = (x0[:, :, None, :] * h[:, None, :, :]).reshape(B, F * G, E)
                y = jax.nn.relu(jnp.einsum('oc,bce->boe', Ws[i], z) + bs[i][None, :, None])
                if i != n_layers - 1:
                    half = y.shape[1] // 2
                    x_keep, h = (y[:, :half, :], y[:, half:, :])
                else:
                    x_keep, h = (y, y)
                xs.append(x_keep)
            return jnp.sum(jnp.concatenate(xs, axis=1), axis=2)
        return _cin_forward(x, [W0, W1, W2], [b0, b1, b2])
    e = jnp.stack([tbl_0[ids[:, 0]], tbl_1[ids[:, 1]], tbl_2[ids[:, 2]], tbl_3[ids[:, 3]], tbl_4[ids[:, 4]], tbl_5[ids[:, 5]], tbl_6[ids[:, 6]], tbl_7[ids[:, 7]], tbl_8[ids[:, 8]], tbl_9[ids[:, 9]], tbl_10[ids[:, 10]], tbl_11[ids[:, 11]], tbl_12[ids[:, 12]], tbl_13[ids[:, 13]], tbl_14[ids[:, 14]], tbl_15[ids[:, 15]], tbl_16[ids[:, 16]], tbl_17[ids[:, 17]], tbl_18[ids[:, 18]], tbl_19[ids[:, 19]], tbl_20[ids[:, 20]], tbl_21[ids[:, 21]], tbl_22[ids[:, 22]], tbl_23[ids[:, 23]], tbl_24[ids[:, 24]], tbl_25[ids[:, 25]], tbl_26[ids[:, 26]], tbl_27[ids[:, 27]], tbl_28[ids[:, 28]], tbl_29[ids[:, 29]], tbl_30[ids[:, 30]], tbl_31[ids[:, 31]]], axis=1)
    z = _L0_rec_ref(e, L0_rec_W0, L0_rec_b0, L0_rec_W1, L0_rec_b1, L0_rec_W2, L0_rec_b2)
    z = z.reshape(z.shape[0], -1)
    h = jnp.concatenate([z, dense_ctx], axis=1)
    h = jnp.maximum(h @ W_top1 + b_top1, 0.0)
    h = jnp.maximum(h @ W_top2 + b_top2, 0.0)
    y = h @ W_top3
    return y

_drawn_inputs = setup_inputs


def setup_inputs(seed=0):
    import zlib

    import numpy as np

    out = dict(_drawn_inputs(seed))
    spreads = {'b_top1': (0.0, 0.363), 'b_top2': (0.0, 0.4)}
    factors = {'tbl_0': 8.0,
     'tbl_1': 8.0,
     'tbl_2': 8.0,
     'tbl_3': 8.0,
     'tbl_4': 8.0,
     'tbl_5': 8.0,
     'tbl_6': 8.0,
     'tbl_7': 8.0,
     'tbl_8': 8.0,
     'tbl_9': 8.0,
     'tbl_10': 8.0,
     'tbl_11': 8.0,
     'tbl_12': 8.0,
     'tbl_13': 8.0,
     'tbl_14': 8.0,
     'tbl_15': 8.0,
     'tbl_16': 8.0,
     'tbl_17': 8.0,
     'tbl_18': 8.0,
     'tbl_19': 8.0,
     'tbl_20': 8.0,
     'tbl_21': 8.0,
     'tbl_22': 8.0,
     'tbl_23': 8.0,
     'tbl_24': 8.0,
     'tbl_25': 8.0,
     'tbl_26': 8.0,
     'tbl_27': 8.0,
     'tbl_28': 8.0,
     'tbl_29': 8.0,
     'tbl_30': 8.0,
     'tbl_31': 8.0,
     'L0_rec_W0': 8.0,
     'L0_rec_W1': 8.0,
     'L0_rec_W2': 8.0,
     'L0_rec_b0': 4.819,
     'L0_rec_b1': 7.103,
     'L0_rec_b2': 7.224}
    for name, (base, spread) in spreads.items():
        noise = np.random.default_rng([zlib.crc32(name.encode()), seed]).standard_normal(out[name].shape)
        drawn = base * np.exp(spread * noise) if base else spread * noise
        out[name] = jnp.asarray(drawn.astype(out[name].dtype))
    for name, factor in factors.items():
        out[name] = (out[name] * factor).astype(out[name].dtype)
    return out
```

```python
from contextlib import ExitStack

import numpy as np
import concourse.bass as bass
from concourse import mybir

F32 = mybir.dt.float32
I32 = mybir.dt.int32
ALU = mybir.AluOpType
ACT = mybir.ActivationFunctionType
AX = mybir.AxisListType

P = 128
B, F, E = 512, 32, 16
O = 128
G = O // 2
D = 16
N1, N2 = 512, 256

Q = P // F
C = 512
BC = C // E
JC = BC // Q
CHUNKS = B // BC
S0 = [0, 8, 1, 9]
T = F * G // P
T0 = 4
TD, QD = 4, 1
GT = 2
REPS = 3
RING = 8
NG = T // GT
NG0 = T0 // GT + 1


def dlrm_tower(nc, ids, base, tables, dense, w0a, w0b, w0d, w1, w2, cin_bias,
               top1, bias1, top2, bias2, top3, scratch, out):
    with ExitStack() as ctx:
        def sb(name, shape, dt=F32):
            return ctx.enter_context(nc.sbuf_tensor(name, shape, dt))

        def ps(name):
            return ctx.enter_context(nc.psum_tensor(name, [P, 512], F32))

        def sem(name):
            return ctx.enter_context(nc.semaphore(name))

        ids_sb = sb("ids_sb", [P, B // Q], I32)
        base_sb = sb("base_sb", [P, B // Q], I32)
        rows_sb = sb("rows_sb", [P, B // Q], I32)
        emb = sb("emb", [P, B // Q, E])
        x_still = sb("x_still", [P, 2, C])
        x_rot = sb("x_rot", [P, 2, T, C])
        prod0 = sb("prod0", [P, T0 + 1, C])
        prod = sb("prod", [P, RING, GT, C])
        w0_sb = sb("w0_sb", [P, T0, O])
        w0t_sb = sb("w0t_sb", [P, T0, O])
        w0d_sb = sb("w0d_sb", [P, O])
        w12_sb = sb("w12_sb", [P, 2, T, O])
        cb_sb = sb("cb_sb", [P, 3])
        top1_sb = sb("top1_sb", [P, 2, N1])
        top1d_sb = sb("top1d_sb", [D, N1])
        top2_sb = sb("top2_sb", [P, N1 // P, N2])
        top3_sb = sb("top3_sb", [P, N2 // P])
        b1_sb = sb("b1_sb", [P, N1 // P])
        b2_sb = sb("b2_sb", [P, N2 // P])
        kept = sb("kept", [P, 3, C])
        feat = sb("feat", [P, 2, B])
        dense_sb = sb("dense_sb", [D, B])
        hid1 = sb("hid1", [P, N1 // P, B])
        hid2 = sb("hid2", [P, N2 // P, B])
        y_sb = sb("y_sb", [1, B])

        y = [ps(f"y{k}") for k in range(3)]
        h = [ps(f"h{k}") for k in range(2)]
        m = [y[0], y[1], ps("m2"), ps("m3")]

        s_ids = sem("s_ids")
        s_rows = sem("s_rows")
        s_gather = [sem("s_gather0"), sem("s_gather1")]
        s_store = sem("s_store")
        s_x = [[sem(f"s_x{a}{b}") for b in range(2)] for a in range(2)]
        s_w0 = sem("s_w0")
        s_w0ready = sem("s_w0ready")
        s_w12 = sem("s_w12")
        s_cb = sem("s_cb")
        s_top = sem("s_top")
        s_made0 = sem("s_made0")
        s_used0 = sem("s_used0")
        s_made = sem("s_made")
        s_used = sem("s_used")
        s_h = [sem("s_h0"), sem("s_h1")]
        s_kept = [sem(f"s_kept{k}") for k in range(3)]
        s_feat = [sem(f"s_feat{k}") for k in range(3)]
        s_m1 = sem("s_m1")
        s_hid1 = sem("s_hid1")
        s_m2 = sem("s_m2")
        s_hid2 = sem("s_hid2")
        s_m3 = sem("s_m3")
        s_ysb = sem("s_ysb")
        s_out = sem("s_out")

        block = ctx.enter_context(nc.Block())

        def over_chunks(eng, step):
            step(0, 0, 0, True, False)
            step(1, 0, 1, False, False)
            with eng.Fori(1, CHUNKS // 2 - 1) as i:
                step(i * 2, i, 0, False, False)
                step(i * 2 + 1, i, 1, False, False)
            step(CHUNKS - 2, CHUNKS // 2 - 1, 0, False, False)
            step(CHUNKS - 1, CHUNKS // 2 - 1, 1, False, True)

        KEEP = [slice(0, G), slice(G, P), slice(0, P)]
        HAND = [slice(G, P), slice(0, G)]
        SHIFT16 = slice(F * QD, F * QD + F)

        def windows(c, row):
            v = scratch[c, row:row + F, :]
            return bass.AP(v.tensor, v.offset, [[C, F], [2 * C, T // 2], [1, C]])

        @block.sync
        def _(sp):
            sp.dma_start(ids_sb[:, :], ids).then_inc(s_ids, 16)
            sp.dma_start(base_sb[:, :], base).then_inc(s_ids, 16)
            sp.dma_start(w0_sb[:, :, :], w0a).then_inc(s_w0, 16)
            sp.dma_start(w0t_sb[:, :, :], w0b).then_inc(s_w0, 16)
            sp.dma_start(w0d_sb[SHIFT16, :], w0d).then_inc(s_w0, 16)
            sp.dma_start(cb_sb[:, :], cin_bias).then_inc(s_cb, 16)

            def fetch(c, i, k, prior):
                sp.wait_ge(s_gather[k], 16 * JC * (i + 1))
                for rep in range(REPS):
                    sp.dma_start(scratch[c, F * rep:F * rep + F, :].rearrange("r (q n) -> q r n", q=Q),
                                 emb[:, bass.ds(c * JC, JC), :].rearrange("p j e -> p (j e)")).then_inc(s_store, 16)
                sp.wait_ge(s_store, 16 * REPS * (c + 1))
                for half in range(2):
                    if prior:
                        sp.wait_ge(s_made, 2 * NG * (c - 1) - (NG // 2 if half == 0 else 0))
                    if half == 0:
                        for q in range(Q):
                            sp.dma_start(x_still[F * q:F * q + F, k, :], scratch[c, 0:F, :]).then_inc(s_x[k][0], 16)
                    for q in (0, 2, 1, 3):
                        t0 = half * (T // 2)
                        sp.dma_start(x_rot[F * q:F * q + F, k, t0:t0 + T // 2, :],
                                     windows(c, S0[q] + 2 * t0)).then_inc(s_x[k][half], 16)

            fetch(0, 0, 0, False)
            sp.dma_start(w12_sb[:, 0, :, :], w1).then_inc(s_w12, 16)
            sp.dma_start(w12_sb[:, 1, :, :], w2).then_inc(s_w12, 16)
            fetch(1, 0, 1, False)
            for dst, src in ((top1_sb[:, :, :], top1[0:2 * P, :].rearrange("(k p) n -> p k n", p=P)),
                             (top1d_sb[:, :], top1[2 * P:, :]),
                             (top2_sb[:, :, :], top2.rearrange("(k p) n -> p k n", p=P)),
                             (top3_sb[:, :], top3), (b1_sb[:, :], bias1), (b2_sb[:, :], bias2),
                             (dense_sb[:, :], dense)):
                sp.dma_start(dst, src).then_inc(s_top, 16)
            with sp.Fori(1, CHUNKS // 2) as i:
                fetch(i * 2, i, 0, True)
                fetch(i * 2 + 1, i, 1, True)
            sp.wait_ge(s_ysb, 1)
            sp.dma_start(out, y_sb[:, :]).then_inc(s_out, 16)
            sp.wait_ge(s_out, 16)

        @block.gpsimd
        def _(pool):
            pool.wait_ge(s_rows, 1)
            for c in range(CHUNKS):
                if c >= 2:
                    pool.wait_ge(s_gather[c % 2], 16 * JC * (c // 2))
                for j in range(c * JC, c * JC + JC):
                    nc.gpsimd.indirect_dma_start(
                        out=emb[:, j, :], out_offset=None, in_=tables,
                        in_offset=bass.IndirectOffsetOnAxis(ap=rows_sb[:, j:j + 1], axis=0),
                    ).then_inc(s_gather[c % 2], 16)

        @block.vector
        def _(dve):
            dve.wait_ge(s_ids, 32)
            nc.vector.tensor_tensor(rows_sb[:, :], ids_sb[:, :], base_sb[:, :], ALU.add).then_inc(s_rows, 1)
            dve.wait_ge(s_w0, 48)
            for part, tiles in ((slice(F, G), slice(0, 1)), (slice(G, P), slice(0, 1)), (slice(0, P), slice(1, T0))):
                nc.vector.tensor_tensor(w0_sb[part, tiles, :], w0_sb[part, tiles, :], w0t_sb[part, tiles, :],
                                        ALU.add).then_inc(s_w0ready, 1)

            def twice(v):
                return v.rearrange("p (a n) -> p a n", a=1).to_broadcast([P, GT, C])

            def layer0(c, i, k, first):
                dve.wait_ge(s_x[k][0], 16 * 2 * Q * (i + 1))
                for g in range(NG0 - 1):
                    if not first:
                        dve.wait_ge(s_used0, NG0 * (c - 1) + g + 1)
                    nc.vector.tensor_tensor(prod0[:, GT * g:GT * g + GT, :], x_rot[:, k, GT * g:GT * g + GT, :],
                                            twice(x_still[:, k, :]), ALU.mult).then_inc(s_made0, 1)
                if not first:
                    dve.wait_ge(s_used0, NG0 * c)
                nc.vector.tensor_tensor(prod0[SHIFT16, T0, :], x_rot[SHIFT16, k, TD, :], x_still[SHIFT16, k, :],
                                        ALU.mult).then_inc(s_made0, 1)

            def make(c, k, layer, g, free):
                if free:
                    dve.wait_ge(s_used, 2 * NG * c + NG * layer + g + 1 - RING)
                nc.vector.tensor_tensor(prod[:, (NG * layer + g) % RING, :, :], x_rot[:, k, GT * g:GT * g + GT, :],
                                        twice(h[layer][:, :]), ALU.mult).then_inc(s_made, 1)

            def sum_lanes(c, layer):
                part = KEEP[layer]
                dve.wait_ge(s_kept[layer], c + 1)
                nc.vector.tensor_reduce(feat[part, layer // 2, bass.ds(c * BC, BC)],
                                        kept[part, layer, :].rearrange("p (b e) -> p b e", e=E),
                                        AX.X, ALU.add).then_inc(s_feat[layer], 1)

            def step(c, i, k, first, last):
                dve.wait_ge(s_h[0], 2 * (c + 1))
                for g in range(NG):
                    if g == NG // 2:
                        dve.wait_ge(s_x[k][1], 16 * Q * (i + 1))
                    make(c, k, 0, g, not first)
                    if g == 1:
                        sum_lanes(c, 0)
                if not last:
                    layer0(c + 1, i + k, 1 - k, False)
                dve.wait_ge(s_h[1], 2 * (c + 1))
                for g in range(NG):
                    make(c, k, 1, g, True)
                    if g == 1:
                        sum_lanes(c, 1)
                sum_lanes(c, 2)

            layer0(0, 0, 0, True)
            over_chunks(dve, step)
            dve.wait_ge(s_m3, 1)
            nc.vector.tensor_copy(y_sb[:, :], m[2][0:1, :]).then_inc(s_ysb, 1)

        @block.scalar
        def _(act):
            act.wait_ge(s_cb, 16)

            def relu(dst, layer, part):
                return nc.scalar.activation(dst, y[layer][part, :], ACT.Relu, bias=cb_sb[part, layer:layer + 1])

            def hand_on(c, layer, first):
                if not first:
                    act.wait_ge(s_made, 2 * NG * (c - 1) + NG * (layer + 1))
                relu(h[layer][0:G, :], layer, HAND[layer]).then_inc(s_h[layer], 1)
                relu(h[layer][G:P, :], layer, HAND[layer]).then_inc(s_h[layer], 1)

            def keep(c, layer, first):
                if not first:
                    act.wait_ge(s_feat[layer], c)
                relu(kept[KEEP[layer], layer, :], layer, KEEP[layer]).then_inc(s_kept[layer], 1)

            def layer0(c, first):
                act.wait_ge(s_used0, NG0 * (c + 1))
                hand_on(c, 0, first)
                keep(c, 0, first)

            def step(c, i, k, first, last):
                act.wait_ge(s_used, 2 * NG * c + NG)
                hand_on(c, 1, first)
                keep(c, 1, first)
                if not last:
                    layer0(c + 1, False)
                act.wait_ge(s_used, 2 * NG * (c + 1))
                keep(c, 2, first)

            layer0(0, True)
            over_chunks(act, step)
            act.wait_ge(s_top, 16 * 7)
            for n in range(N1 // P):
                act.wait_ge(s_m1, n + 1)
                nc.scalar.activation(hid1[:, n, :], m[n][:, :], ACT.Relu, bias=b1_sb[:, n:n + 1]).then_inc(s_hid1, 1)
            for n in range(N2 // P):
                act.wait_ge(s_m2, n + 1)
                nc.scalar.activation(hid2[:, n, :], m[n][:, :], ACT.Relu, bias=b2_sb[:, n:n + 1]).then_inc(s_hid2, 1)

        @block.tensor
        def _(pe):
            def layer0(c, first):
                if not first:
                    pe.wait_ge(s_kept[0], c)
                for g in range(NG0 - 1):
                    pe.wait_ge(s_made0, NG0 * c + g + 1)
                    for t in range(GT * g, GT * g + GT):
                        mm = nc.tensor.matmul(y[0][:, :], w0_sb[:, t, :], prod0[:, t, :], start=t == 0, stop=False)
                    mm.then_inc(s_used0, 1)
                pe.wait_ge(s_made0, NG0 * (c + 1))
                nc.tensor.matmul(y[0][:, :], w0d_sb[SHIFT16, :], prod0[SHIFT16, T0, :],
                                 start=False, stop=True).then_inc(s_used0, 1)

            def layer(c, n, first):
                if not first:
                    pe.wait_ge(s_kept[n], c)
                for g in range(NG):
                    pe.wait_ge(s_made, 2 * NG * c + NG * (n - 1) + g + 1)
                    for t in range(GT):
                        mm = nc.tensor.matmul(y[n][:, :], w12_sb[:, n - 1, GT * g + t, :],
                                              prod[:, (NG * (n - 1) + g) % RING, t, :],
                                              start=g == 0 and t == 0, stop=g == NG - 1 and t == GT - 1)
                    mm.then_inc(s_used, 1)

            def step(c, i, k, first, last):
                layer(c, 1, first)
                if not last:
                    layer0(c + 1, False)
                layer(c, 2, first)

            pe.wait_ge(s_w0ready, 3)
            layer0(0, True)
            pe.wait_ge(s_w12, 32)
            over_chunks(pe, step)

            pe.wait_ge(s_top, 16 * 7)
            for layer_ in range(3):
                pe.wait_ge(s_feat[layer_], CHUNKS)
                pe.wait_ge(s_kept[layer_], CHUNKS)
            for n in range(N1 // P):
                cols = slice(P * n, P * n + P)
                nc.tensor.matmul(m[n][:, :], top1_sb[:, 0, cols], feat[:, 0, :], start=True, stop=False)
                nc.tensor.matmul(m[n][:, :], top1_sb[:, 1, cols], feat[:, 1, :], start=False, stop=False)
                nc.tensor.matmul(m[n][:, :], top1d_sb[:, cols], dense_sb[:, :],
                                 start=False, stop=True).then_inc(s_m1, 1)
            for n in range(N2 // P):
                for k in range(N1 // P):
                    pe.wait_ge(s_hid1, max(k, n) + 1)
                    mm = nc.tensor.matmul(m[n][:, :], top2_sb[:, k, P * n:P * n + P], hid1[:, k, :],
                                          start=k == 0, stop=k == N1 // P - 1)
                mm.then_inc(s_m2, 1)
            for k in range(N2 // P):
                pe.wait_ge(s_hid2, k + 1)
                pe.wait_ge(s_hid1, N1 // P)
                mm = nc.tensor.matmul(m[2][0:1, :], top3_sb[:, k:k + 1], hid2[:, k, :],
                                      start=k == 0, stop=k == N2 // P - 1)
            mm.then_inc(s_m3, 1)


def kernel(**inputs):
    import concourse.bacc as bacc
    from concourse.bass_utils import run_bass_kernel_spmd

    a = {k: np.asarray(v) for k, v in inputs.items()}
    tables = [a[f"tbl_{f}"] for f in range(F)]
    first_row = np.cumsum([0] + [t.shape[0] for t in tables[:-1]]).astype(np.int32)

    p = np.arange(P)
    shift = np.array(S0)[p // F][:, None] + 2 * np.arange(T)[None, :]
    f12 = (shift + (p % F)[:, None]) % F
    pair12 = f12 * G + (p % G)[:, None]
    r0 = (p % F)[:, None] + 0 * f12[:, :T0]
    w0 = a["L0_rec_W0"].T
    w1 = np.roll(a["L0_rec_W1"], G, axis=0).T
    b1 = np.roll(a["L0_rec_b1"], G)
    arrays = {
        "ids": a["ids"].reshape(CHUNKS, Q, JC, F).transpose(1, 3, 0, 2).reshape(P, B // Q),
        "base": np.repeat(np.tile(first_row, Q)[:, None], B // Q, axis=1),
        "tables": np.concatenate(tables, axis=0),
        "dense": a["dense_ctx"].T,
        "w0a": w0[r0 * F + f12[:, :T0]],
        "w0b": w0[f12[:, :T0] * F + r0],
        "w0d": w0[np.arange(F) * F + (np.arange(F) + F // 2) % F],
        "w1": w1[pair12],
        "w2": a["L0_rec_W2"].T[pair12],
        "cin_bias": np.stack([a["L0_rec_b0"], b1, a["L0_rec_b2"]], axis=1),
        "top1": a["W_top1"],
        "bias1": a["b_top1"].reshape(N1 // P, P).T,
        "top2": a["W_top2"],
        "bias2": a["b_top2"].reshape(N2 // P, P).T,
        "top3": a["W_top3"].reshape(N2 // P, P).T,
    }
    nc = bacc.Bacc("TRN2", target_bir_lowering=False, num_devices=1)
    feeds, args = {}, []
    for name, v in arrays.items():
        v = np.ascontiguousarray(v)
        feeds[f"in_{name}"] = v
        args.append(nc.dram_tensor(f"in_{name}", v.shape, mybir.dt.from_np(v.dtype), kind="ExternalInput").ap())
    args.append(nc.dram_tensor("scratch", (CHUNKS, REPS * F, C), F32, kind="Internal").ap())
    args.append(nc.dram_tensor("out_y", (1, B), F32, kind="ExternalOutput").ap())
    dlrm_tower(nc, *args)
    r = run_bass_kernel_spmd(nc, [feeds], core_ids=[0])
    return r.results[0]["out_y"].reshape(B, 1)
```

```python
from contextlib import ExitStack

import numpy as np
import concourse.bass as bass
from concourse import mybir

F32 = mybir.dt.float32
F32R = mybir.dt.float32r
I32 = mybir.dt.int32
ALU = mybir.AluOpType
ACT = mybir.ActivationFunctionType
AX = mybir.AxisListType

P = 128
B, F, E = 512, 32, 16
O = 128
G = O // 2
D = 16
N1, N2 = 512, 256

Q = P // F
C = 512
BC = C // E
JC = BC // Q
CHUNKS = B // BC
S0 = [0, 8, 1, 9]
T = F * G // P
T0 = 4
TD, QD = 4, 1
REPS = 3

GT = 2
NG = T // GT
NG0 = T0 // GT + 1
PLAIN = [g for g in range(NG) if g % 2 == 0]
SPLIT = [g for g in range(NG) if g % 2 == 1]
NP, NS = len(PLAIN), len(SPLIT)
USE = [0, 2, 1, 4, 3, 6, 5, 7]
PLAIN_RING = 4
ROUGH_RING = 2
PARTS_RING = 4
assert sorted(USE) == sorted(PLAIN + SPLIT) == list(range(NG)) and NG - 1 in SPLIT and NG // 2 - 1 in SPLIT
assert 2 * NP % PLAIN_RING == 2 * NS % ROUGH_RING == 2 * NS % PARTS_RING == 0
LOTS = [(0, (CHUNKS - 2) * BC), ((CHUNKS - 2) * BC, B)]



def used(c, layer, g):
    return 2 * NG * c + NG * layer + USE.index(g) + 1


def plain(c, layer, k):
    return 2 * NP * c + NP * layer + k + 1


def split(c, layer, k):
    return 2 * NS * c + NS * layer + k + 1


def before(groups, ring, layer, k):
    n = len(groups) * layer + k - ring
    return (0 if n >= 0 else 1, *divmod(n % (2 * len(groups)), len(groups)))


def dlrm_tower(nc, ids, base, tables, dense, w0a, w0b, w0d, w_plain, w_split, cin_bias,
               top1, bias1, top2, bias2, top3, scratch, out):
    with ExitStack() as ctx:
        def sb(name, shape, dt=F32):
            return ctx.enter_context(nc.sbuf_tensor(name, shape, dt))

        def ps(name):
            return ctx.enter_context(nc.psum_tensor(name, [P, 512], F32))

        def sem(name):
            return ctx.enter_context(nc.semaphore(name))

        ids_sb = sb("ids_sb", [P, B // Q], I32)
        base_sb = sb("base_sb", [P, JC], I32)
        rows_sb = sb("rows_sb", [P, 2, JC], I32)
        emb = sb("emb", [P, 2, JC, E])
        x_still = sb("x_still", [P, 2, C])
        x_rot = sb("x_rot", [P, 2, T, C])
        prod0 = sb("prod0", [P, T0 + 1, C])
        prod = sb("prod", [P, PLAIN_RING, GT, C])
        rough = sb("rough", [P, ROUGH_RING, GT, C])
        high = sb("high", [P, PARTS_RING, GT, C], F32R)
        low = sb("low", [P, PARTS_RING, GT, C], F32R)
        w0_sb = sb("w0_sb", [P, T0, O])
        w0t_sb = sb("w0t_sb", [P, T0, O])
        w0d_sb = sb("w0d_sb", [P, O])
        wp_sb = sb("wp_sb", [P, 2, NP, GT, O])
        w_high = sb("w_high", [P, 2, NS, GT, O], F32R)
        w_low = sb("w_low", [P, 2, NS, GT, O], F32R)
        w_stage = x_rot[:, 1, T - 2 * NS * GT * O // C:, :].rearrange("p t n -> p (t n)")
        cb_sb = sb("cb_sb", [P, 3])
        top1_sb = sb("top1_sb", [P, 2, N1])
        top1d_sb = sb("top1d_sb", [D, N1])
        top2_sb = sb("top2_sb", [P, N1 // P, N2])
        top3_sb = sb("top3_sb", [P, N2 // P])
        b1_sb = sb("b1_sb", [P, N1 // P])
        b2_sb = sb("b2_sb", [P, N2 // P])
        kept = sb("kept", [P, 2, C])
        feat = sb("feat", [P, 2, B])
        dense_sb = sb("dense_sb", [D, B])
        hid1 = sb("hid1", [P, N1 // P, LOTS[0][1]])
        hid2 = sb("hid2", [P, N2 // P, LOTS[0][1]])
        y_sb = sb("y_sb", [1, B])

        y = [ps(f"y{k}") for k in range(3)]
        h = [ps(f"h{k}") for k in range(2)]
        m = [ps(f"m{k}") for k in range(3)]

        s_ids = sem("s_ids")
        s_rows = sem("s_rows")
        s_gather = [sem("s_gather0"), sem("s_gather1")]
        s_store = sem("s_store")
        s_x = [[sem(f"s_x{a}{b}") for b in range(2)] for a in range(2)]
        s_w0 = sem("s_w0")
        s_w0ready = sem("s_w0ready")
        s_wp = sem("s_wp")
        s_stage = sem("s_stage")
        s_whigh = sem("s_whigh")
        s_wlow = sem("s_wlow")
        s_cb = sem("s_cb")
        s_top = sem("s_top")
        s_made0 = sem("s_made0")
        s_used0 = sem("s_used0")
        s_plain = sem("s_plain")
        s_rough = sem("s_rough")
        s_high = sem("s_high")
        s_low = sem("s_low")
        s_used = sem("s_used")
        s_h = [sem("s_h0"), sem("s_h1")]
        s_kept = [sem(f"s_kept{k}") for k in range(3)]
        s_feat = [sem(f"s_feat{k}") for k in range(3)]
        s_m1 = sem("s_m1")
        s_hid1 = sem("s_hid1")
        s_m2 = sem("s_m2")
        s_hid2 = sem("s_hid2")
        s_m3 = sem("s_m3")
        s_ysb = sem("s_ysb")
        s_out = sem("s_out")

        block = ctx.enter_context(nc.Block())

        def over_chunks(eng, step):
            step(0, 0, 0, True, None)
            step(1, 0, 1, False, None)
            with eng.Fori(1, CHUNKS // 2 - 1) as i:
                step(i * 2, i, 0, False, None)
                step(i * 2 + 1, i, 1, False, None)
            step(CHUNKS - 2, CHUNKS // 2 - 1, 0, False, 0)
            step(CHUNKS - 1, CHUNKS // 2 - 1, 1, False, 1)

        KEEP = [slice(0, G), slice(G, P), slice(0, P)]
        HAND = [slice(G, P), slice(0, G)]
        SHIFT16 = slice(F * QD, F * QD + F)

        def windows(c, row, tiles):
            v = scratch[c, row:row + F, :]
            return bass.AP(v.tensor, v.offset, [[C, F], [2 * C, tiles], [1, C]])

        @block.sync
        def _(sp):
            sp.dma_start(ids_sb[:, :], ids).then_inc(s_ids, 16)
            sp.dma_start(base_sb[:, :], base).then_inc(s_ids, 16)
            sp.dma_start(w0_sb[:, :, :], w0a).then_inc(s_w0, 16)
            sp.dma_start(w0t_sb[:, :, :], w0b).then_inc(s_w0, 16)
            sp.dma_start(w0d_sb[SHIFT16, :], w0d).then_inc(s_w0, 16)
            sp.dma_start(cb_sb[:, :], cin_bias).then_inc(s_cb, 16)
            sp.dma_start(w_stage, w_split).then_inc(s_stage, 16)
            sp.dma_start(wp_sb[:, :, :, :, :], w_plain).then_inc(s_wp, 16)

            def fetch(c, i, k, prior):
                sp.wait_ge(s_gather[k], 16 * JC * (i + 1))
                for rep in range(REPS):
                    sp.dma_start(scratch[c, F * rep:F * rep + F, :].rearrange("r (q n) -> q r n", q=Q),
                                 emb[:, k, :, :].rearrange("p j e -> p (j e)")).then_inc(s_store, 16)
                sp.wait_ge(s_store, 16 * REPS * (c + 1))
                for half in range(2):
                    if prior:
                        sp.wait_ge(s_rough, split(c - 2, 1, (half + 1) * NS // 2 - 1))
                    if half == 0:
                        for q in range(Q):
                            sp.dma_start(x_still[F * q:F * q + F, k, :], scratch[c, 0:F, :]).then_inc(s_x[k][0], 16)
                    if not prior and k == 1 and half == 1:
                        sp.wait_ge(s_wlow, 1)
                    for q in (0, 2, 1, 3):
                        t0 = half * (T // 2)
                        sp.dma_start(x_rot[F * q:F * q + F, k, t0:t0 + T // 2, :],
                                     windows(c, S0[q] + 2 * t0, T // 2)).then_inc(s_x[k][half], 16)

            fetch(0, 0, 0, False)
            fetch(1, 0, 1, False)
            for dst, src in ((top1_sb[:, :, :], top1[0:2 * P, :].rearrange("(k p) n -> p k n", p=P)),
                             (top1d_sb[:, :], top1[2 * P:, :]),
                             (top2_sb[:, :, :], top2.rearrange("(k p) n -> p k n", p=P)),
                             (top3_sb[:, :], top3), (b1_sb[:, :], bias1), (b2_sb[:, :], bias2),
                             (dense_sb[:, :], dense)):
                sp.dma_start(dst, src).then_inc(s_top, 16)
            with sp.Fori(1, CHUNKS // 2) as i:
                fetch(i * 2, i, 0, True)
                fetch(i * 2 + 1, i, 1, True)
            sp.wait_ge(s_ysb, len(LOTS))
            sp.dma_start(out, y_sb[:, :]).then_inc(s_out, 16)
            sp.wait_ge(s_out, 16)

        @block.gpsimd
        def _(pool):
            def number_rows(c, k, prior):
                if prior:
                    pool.wait_ge(s_store, 16 * REPS * (c - 1))
                nc.gpsimd.tensor_tensor(rows_sb[:, k, :], ids_sb[:, bass.ds(c * JC, JC)], base_sb[:, :],
                                        ALU.add).then_inc(s_rows, 1)

            def look_up(k):
                for j in range(JC):
                    nc.gpsimd.indirect_dma_start(
                        out=emb[:, k, j, :], out_offset=None, in_=tables,
                        in_offset=bass.IndirectOffsetOnAxis(ap=rows_sb[:, k, j:j + 1], axis=0),
                    ).then_inc(s_gather[k], 16)

            def take_low(c, layer, n):
                at = (NS * layer + n) % PARTS_RING
                pool.wait_ge(s_high, split(c, layer, n))
                nc.gpsimd.tensor_tensor(low[:, at, :, :], rough[:, (NS * layer + n) % ROUGH_RING, :, :],
                                        high[:, at, :, :].bitcast(F32), ALU.subtract).then_inc(s_low, 1)

            def step(c, i, k, first, lot):
                if lot is None:
                    number_rows(c + 2, k, True)
                for n in range(NS):
                    if lot is None and n == NS - 1:
                        pool.wait_ge(s_rows, c + 3)
                    take_low(c, 0, n)
                if lot is None:
                    look_up(k)
                for n in range(NS):
                    take_low(c, 1, n)

            pool.wait_ge(s_ids, 32)
            for c in range(2):
                number_rows(c, c, False)
                pool.wait_ge(s_rows, c + 1)
                look_up(c)
            over_chunks(pool, step)

        @block.vector
        def _(dve):
            dve.wait_ge(s_w0, 48)
            for part, tiles in ((slice(F, G), slice(0, 1)), (slice(G, P), slice(0, 1)), (slice(0, P), slice(1, T0))):
                nc.vector.tensor_tensor(w0_sb[part, tiles, :], w0_sb[part, tiles, :], w0t_sb[part, tiles, :],
                                        ALU.add).then_inc(s_w0ready, 1)
            dve.wait_ge(s_whigh, 1)
            nc.vector.tensor_tensor(w_low[:, :, :, :, :].rearrange("p l k t o -> p (l k t o)"), w_stage,
                                    w_high[:, :, :, :, :].rearrange("p l k t o -> p (l k t o)").bitcast(F32),
                                    ALU.subtract).then_inc(s_wlow, 1)

            def twice(v):
                return v.rearrange("p (a n) -> p a n", a=1).to_broadcast([P, GT, C])

            def layer0(c, i, k, first):
                dve.wait_ge(s_x[k][0], 16 * 2 * Q * (i + 1))
                for g in range(NG0 - 1):
                    if not first:
                        dve.wait_ge(s_used0, NG0 * (c - 1) + g + 1)
                    nc.vector.tensor_tensor(prod0[:, GT * g:GT * g + GT, :], x_rot[:, k, GT * g:GT * g + GT, :],
                                            twice(x_still[:, k, :]), ALU.mult).then_inc(s_made0, 1)
                if not first:
                    dve.wait_ge(s_used0, NG0 * c)
                nc.vector.tensor_tensor(prod0[SHIFT16, T0, :], x_rot[SHIFT16, k, TD, :], x_still[SHIFT16, k, :],
                                        ALU.mult).then_inc(s_made0, 1)

            def make(c, k, layer, g, first):
                if g in PLAIN:
                    n = PLAIN.index(g)
                    back, l, j = before(PLAIN, PLAIN_RING, layer, n)
                    dst, done = prod[:, (NP * layer + n) % PLAIN_RING, :, :], s_plain
                    if not (first and back):
                        dve.wait_ge(s_used, used(c - back, l, PLAIN[j]))
                else:
                    n = SPLIT.index(g)
                    back, l, j = before(SPLIT, ROUGH_RING, layer, n)
                    dst, done = rough[:, (NS * layer + n) % ROUGH_RING, :, :], s_rough
                    if not (first and back):
                        dve.wait_ge(s_low, split(c - back, l, j))
                nc.vector.tensor_tensor(dst, x_rot[:, k, GT * g:GT * g + GT, :],
                                        twice(h[layer][:, :]), ALU.mult).then_inc(done, 1)

            def sum_lanes(c, layer):
                part = KEEP[layer]
                dve.wait_ge(s_kept[layer], c + 1)
                nc.vector.tensor_reduce(feat[part, layer // 2, bass.ds(c * BC, BC)],
                                        kept[part, layer // 2, :].rearrange("p (b e) -> p b e", e=E),
                                        AX.X, ALU.add).then_inc(s_feat[layer], 1)

            def scores(lot):
                a, b = LOTS[lot]
                dve.wait_ge(s_m3, lot + 1)
                nc.vector.tensor_copy(y_sb[:, a:b], m[2][0:1, 0:b - a]).then_inc(s_ysb, 1)

            def step(c, i, k, first, lot):
                dve.wait_ge(s_h[0], 2 * (c + 1))
                for g in range(NG):
                    if g == NG // 2:
                        dve.wait_ge(s_x[k][1], 16 * Q * (i + 1))
                    make(c, k, 0, g, first)
                    if g == NG // 2 and not first:
                        sum_lanes(c - 1, 2)
                    if g == NG // 2 + 1:
                        sum_lanes(c, 0)
                if lot != 1:
                    layer0(c + 1, i + k, 1 - k, False)
                dve.wait_ge(s_h[1], 2 * (c + 1))
                for g in range(NG):
                    make(c, k, 1, g, first)
                    if g == NG // 2:
                        sum_lanes(c, 1)
                if lot == 1:
                    scores(0)
                    sum_lanes(c, 2)

            layer0(0, 0, 0, True)
            over_chunks(dve, step)
            scores(1)

        @block.scalar
        def _(act):
            act.wait_ge(s_stage, 16)
            nc.scalar.activation(w_high[:, :, :, :, :].rearrange("p l k t o -> p (l k t o)"), w_stage,
                                 ACT.Copy).then_inc(s_whigh, 1)
            act.wait_ge(s_cb, 16)

            def relu(dst, layer, part):
                return nc.scalar.activation(dst, y[layer][part, :], ACT.Relu, bias=cb_sb[part, layer:layer + 1])

            def hand_on(c, layer, first):
                if not first:
                    act.wait_ge(s_rough, split(c - 1, layer, NS - 1))
                relu(h[layer][0:G, :], layer, HAND[layer]).then_inc(s_h[layer], 1)
                relu(h[layer][G:P, :], layer, HAND[layer]).then_inc(s_h[layer], 1)

            def keep(c, layer, first):
                if not first:
                    act.wait_ge(s_feat[layer], c)
                relu(kept[KEEP[layer], layer // 2, :], layer, KEEP[layer]).then_inc(s_kept[layer], 1)

            def layer0(c, first):
                act.wait_ge(s_used0, NG0 * (c + 1))
                hand_on(c, 0, first)
                keep(c, 0, first)

            def round_high(c, layer, n, first):
                back, l, j = before(SPLIT, PARTS_RING, layer, n)
                if not (first and back):
                    act.wait_ge(s_used, used(c - back, l, SPLIT[j]))
                act.wait_ge(s_rough, split(c, layer, n))
                nc.scalar.activation(high[:, (NS * layer + n) % PARTS_RING, :, :],
                                     rough[:, (NS * layer + n) % ROUGH_RING, :, :], ACT.Copy).then_inc(s_high, 1)

            def hidden(lot, n, s_m, hid, bias, s_hid, tiles):
                a, b = LOTS[lot]
                act.wait_ge(s_m, tiles * lot + n + 1)
                nc.scalar.activation(hid[:, n, 0:b - a], m[n % 2][:, 0:b - a], ACT.Relu,
                                     bias=bias[:, n:n + 1]).then_inc(s_hid, 1)

            def hidden1(lot, n):
                hidden(lot, n, s_m1, hid1, b1_sb, s_hid1, N1 // P)

            def hidden2(lot, n):
                hidden(lot, n, s_m2, hid2, b2_sb, s_hid2, N2 // P)

            def step(c, i, k, first, lot):
                if first:
                    round_high(c, 0, 0, first)
                for n in range(1, NS):
                    round_high(c, 0, n, first)
                    if lot == 1 and n < 3:
                        hidden2(0, n - 1)
                act.wait_ge(s_used, 2 * NG * c + NG)
                hand_on(c, 1, first)
                keep(c, 1, first)
                round_high(c, 1, 0, first)
                if lot != 1:
                    layer0(c + 1, False)
                if lot == 0:
                    act.wait_ge(s_top, 16 * 7)
                    hidden1(0, 0)
                for n in range(1, NS):
                    round_high(c, 1, n, first)
                    if lot == 0:
                        hidden1(0, n)
                if lot != 1:
                    round_high(c + 1, 0, 0, False)
                act.wait_ge(s_used, 2 * NG * (c + 1))
                keep(c, 2, first)

            layer0(0, True)
            over_chunks(act, step)
            for n in range(N1 // P):
                hidden1(1, n)
            for n in range(N2 // P):
                hidden2(1, n)

        @block.tensor
        def _(pe):
            def layer0(c, first):
                if not first:
                    pe.wait_ge(s_kept[0], c)
                for g in range(NG0 - 1):
                    pe.wait_ge(s_made0, NG0 * c + g + 1)
                    for t in range(GT * g, GT * g + GT):
                        mm = nc.tensor.matmul(y[0][:, :], w0_sb[:, t, :], prod0[:, t, :], start=t == 0, stop=False)
                    mm.then_inc(s_used0, 1)
                pe.wait_ge(s_made0, NG0 * (c + 1))
                nc.tensor.matmul(y[0][:, :], w0d_sb[SHIFT16, :], prod0[SHIFT16, T0, :],
                                 start=False, stop=True).then_inc(s_used0, 1)

            def layer(c, l, first):
                total = y[l + 1][:, :]
                if not first:
                    pe.wait_ge(s_kept[l + 1], c)
                for g in USE:
                    start, stop = g == USE[0], g == USE[-1]
                    if g in PLAIN:
                        n = PLAIN.index(g)
                        pe.wait_ge(s_plain, plain(c, l, n))
                        for t in range(GT):
                            mm = nc.tensor.matmul(total, wp_sb[:, l, n, t, :],
                                                  prod[:, (NP * l + n) % PLAIN_RING, t, :],
                                                  start=start and t == 0, stop=stop and t == GT - 1)
                    else:
                        n = SPLIT.index(g)
                        at = (NS * l + n) % PARTS_RING
                        pe.wait_ge(s_low, split(c, l, n))
                        for t in range(GT):
                            hi, lo = w_high[:, l, n, t, :], w_low[:, l, n, t, :]
                            nc.tensor.matmul(total, hi, high[:, at, t, :], start=start and t == 0, stop=False)
                            nc.tensor.matmul(total, hi, low[:, at, t, :], start=False, stop=False)
                            mm = nc.tensor.matmul(total, lo, high[:, at, t, :], start=False,
                                                  stop=stop and t == GT - 1)
                    mm.then_inc(s_used, 1)

            def mlp1(lot):
                a, b = LOTS[lot]
                for k in range(3):
                    pe.wait_ge(s_feat[k], b // BC)
                for n in range(N1 // P):
                    if n >= 2 or lot:
                        pe.wait_ge(s_hid1, N1 // P * lot + n - 1)
                    if lot and n < 2:
                        pe.wait_ge(s_hid2, n + 1)
                    cols, total = slice(P * n, P * n + P), m[n % 2][:, 0:b - a]
                    nc.tensor.matmul(total, top1_sb[:, 0, cols], feat[:, 0, a:b], start=True, stop=False)
                    nc.tensor.matmul(total, top1_sb[:, 1, cols], feat[:, 1, a:b], start=False, stop=False)
                    nc.tensor.matmul(total, top1d_sb[:, cols], dense_sb[:, a:b],
                                     start=False, stop=True).then_inc(s_m1, 1)

            def mlp2(lot):
                a, b = LOTS[lot]
                for n in range(N2 // P):
                    for k in range(N1 // P):
                        pe.wait_ge(s_hid1, N1 // P * lot + (k + 1 if n else N1 // P))
                        mm = nc.tensor.matmul(m[n][:, 0:b - a], top2_sb[:, k, P * n:P * n + P], hid1[:, k, 0:b - a],
                                              start=k == 0, stop=k == N1 // P - 1)
                    mm.then_inc(s_m2, 1)

            def mlp3(lot):
                a, b = LOTS[lot]
                if lot:
                    pe.wait_ge(s_ysb, lot)
                for k in range(N2 // P):
                    pe.wait_ge(s_hid2, N2 // P * lot + k + 1)
                    mm = nc.tensor.matmul(m[2][0:1, 0:b - a], top3_sb[:, k:k + 1], hid2[:, k, 0:b - a],
                                          start=k == 0, stop=k == N2 // P - 1)
                mm.then_inc(s_m3, 1)

            def step(c, i, k, first, lot):
                if lot == 1:
                    mlp2(0)
                layer(c, 0, first)
                if lot != 1:
                    layer0(c + 1, False)
                if lot == 0:
                    pe.wait_ge(s_top, 16 * 7)
                    mlp1(0)
                if lot == 1:
                    mlp3(0)
                layer(c, 1, first)

            pe.wait_ge(s_w0ready, 3)
            layer0(0, True)
            pe.wait_ge(s_wp, 16)
            pe.wait_ge(s_wlow, 1)
            over_chunks(pe, step)
            mlp1(1)
            mlp2(1)
            mlp3(1)


def kernel(**inputs):
    import concourse.bacc as bacc
    from concourse.bass_utils import run_bass_kernel_spmd

    a = {k: np.asarray(v) for k, v in inputs.items()}
    tables = [a[f"tbl_{f}"] for f in range(F)]
    first_row = np.cumsum([0] + [t.shape[0] for t in tables[:-1]]).astype(np.int32)

    p = np.arange(P)
    shift = np.array(S0)[p // F][:, None] + 2 * np.arange(T)[None, :]
    f12 = (shift + (p % F)[:, None]) % F
    pair12 = f12 * G + (p % G)[:, None]
    r0 = (p % F)[:, None] + 0 * f12[:, :T0]
    w0 = a["L0_rec_W0"].T
    w1 = np.roll(a["L0_rec_W1"], G, axis=0).T
    b1 = np.roll(a["L0_rec_b1"], G)
    w12 = np.stack([w1[pair12], a["L0_rec_W2"].T[pair12]], axis=1).reshape(P, 2, NG, GT, O)
    arrays = {
        "ids": a["ids"].reshape(CHUNKS, Q, JC, F).transpose(1, 3, 0, 2).reshape(P, B // Q),
        "base": np.repeat(np.tile(first_row, Q)[:, None], JC, axis=1),
        "tables": np.concatenate(tables, axis=0),
        "dense": a["dense_ctx"].T,
        "w0a": w0[r0 * F + f12[:, :T0]],
        "w0b": w0[f12[:, :T0] * F + r0],
        "w0d": w0[np.arange(F) * F + (np.arange(F) + F // 2) % F],
        "w_plain": w12[:, :, PLAIN],
        "w_split": w12[:, :, SPLIT].reshape(P, 2 * NS * GT * O),
        "cin_bias": np.stack([a["L0_rec_b0"], b1, a["L0_rec_b2"]], axis=1),
        "top1": a["W_top1"],
        "bias1": a["b_top1"].reshape(N1 // P, P).T,
        "top2": a["W_top2"],
        "bias2": a["b_top2"].reshape(N2 // P, P).T,
        "top3": a["W_top3"].reshape(N2 // P, P).T,
    }
    nc = bacc.Bacc("TRN2", target_bir_lowering=False, num_devices=1)
    feeds, args = {}, []
    for name, v in arrays.items():
        v = np.ascontiguousarray(v)
        feeds[f"in_{name}"] = v
        args.append(nc.dram_tensor(f"in_{name}", v.shape, mybir.dt.from_np(v.dtype), kind="ExternalInput").ap())
    args.append(nc.dram_tensor("scratch", (CHUNKS, REPS * F, C), F32, kind="Internal").ap())
    args.append(nc.dram_tensor("out_y", (1, B), F32, kind="ExternalOutput").ap())
    dlrm_tower(nc, *args)
    r = run_bass_kernel_spmd(nc, [feeds], core_ids=[0])
    return r.results[0]["out_y"].reshape(B, 1)
```

```python
from contextlib import ExitStack

import numpy as np
import concourse.bass as bass
from concourse import mybir

F32 = mybir.dt.float32
F32R = mybir.dt.float32r
I32 = mybir.dt.int32
ALU = mybir.AluOpType
ACT = mybir.ActivationFunctionType
AX = mybir.AxisListType

P = 128
B, F, E = 512, 32, 16
O = 128
G = O // 2
D = 16
N1, N2 = 512, 256

Q = P // F
C = 512
BC = C // E
JC = BC // Q
CHUNKS = B // BC
S0 = [0, 8, 1, 9]
T = F * G // P
T0 = 4
TD, QD = 4, 1
REPS = 3

GT = 2
NG = T // GT
NG0 = T0 // GT + 1
KINDS = ["SPSDSSDP", "SPDSPSDS"]
USE = [[1, 0, 3, 2, 4, 7, 5, 6], [1, 2, 0, 3, 4, 6, 5, 7]]
ALL = [(layer, g) for layer in range(2) for g in range(NG)]
OF = {kind: [x for x in ALL if KINDS[x[0]][x[1]] == kind] for kind in "PSD"}
SPLIT = [x for x in ALL if x not in OF["P"]]
TAKEN = {"P": OF["P"][:KINDS[0].count("P")] + [(-1, g) for g in range(T0 // GT)] + OF["P"][KINDS[0].count("P"):],
         "S": OF["S"], "D": OF["D"]}
RING = {"P": 3,
        "rough S": 4,
        "rough D": 1,
        "parts S": 4,
        "parts D": 1}
assert all(sorted(order) == list(range(NG)) for order in USE)
assert all(len(TAKEN[buf[-1]]) % n == 0 for buf, n in RING.items())
EARLY = 3
SLOTS = 3
STEPS = CHUNKS + 1
LAST_STEP = STEPS - 1
assert (STEPS - 5) % SLOTS == 0
PART = 6
PART_0 = 8
assert max(S0) + 2 * (PART_0 - 1) + F <= 2 * F
LOTS = [(0, (CHUNKS - 2) * BC), ((CHUNKS - 2) * BC, B)]
LAST = LOTS[1][1] - LOTS[1][0]
MLP_AFTER = CHUNKS - 3
assert LOTS[0][1] == (MLP_AFTER + 1) * BC



def kind_of(layer, g):
    return KINDS[layer][g]


def slot(buf, layer, g):
    return TAKEN[buf[-1]].index((layer, g)) % RING[buf]


def last_user(buf, s, edge, layer, g):
    order, ring = TAKEN[buf[-1]], RING[buf]
    n = order.index((layer, g))
    while True:
        n -= ring
        back, (l, j) = -(n // len(order)), order[n % len(order)]
        if edge is None or 0 <= edge - back - l < CHUNKS:
            return s - back - l, l, j
        if edge - back < -1:
            return None


def made(c, layer, g):
    return NG * c + g + 1


def used(c, layer, g):
    if layer == -1:
        return NG0 * c + g + 1
    return NG * c + USE[layer].index(g) + 1


def high_done(c, layer, g):
    same = [j for l, j in SPLIT if l == layer]
    return len(same) * c + same.index(g) + 1


def low_done(c, layer, g):
    same = [j for l, j in OF[kind_of(layer, g)] if l == layer]
    return len(same) * c + same.index(g) + 1


def dlrm_tower(nc, ids, tables, dense, w0a, w0b, w0d, w_plain, w_split, cin_bias,
               top1, top1d, top2, bias2, top3, scratch, out):
    with ExitStack() as ctx:
        def sb(name, shape, dt=F32):
            return ctx.enter_context(nc.sbuf_tensor(name, shape, dt))

        def ps(name):
            return ctx.enter_context(nc.psum_tensor(name, [P, 512], F32))

        def sem(name):
            return ctx.enter_context(nc.semaphore(name))

        ids_sb = sb("ids_sb", [P, B // Q + JC], I32)
        base_sb = ids_sb[:, B // Q:]
        rows_sb = sb("rows_sb", [P, SLOTS, JC], I32)
        emb = sb("emb", [P, SLOTS, JC, E])
        x_still = sb("x_still", [P, C])
        x_rot = sb("x_rot", [P, SLOTS, T, C])
        prod = sb("prod", [P, RING["P"], GT, C])
        rough = sb("rough", [P, RING["rough S"], GT, C])
        high = {kind: sb(f"high_{kind}", [P, RING[f"parts {kind}"], GT, C], F32R) for kind in "SD"}
        low = {kind: sb(f"low_{kind}", [P, RING[f"parts {kind}"], GT, C], F32R) for kind in "SD"}
        w0_sb = sb("w0_sb", [P, T0, O])
        w0d_sb = sb("w0d_sb", [P, O])
        wp_sb = sb("wp_sb", [P, len(OF["P"]), GT, O])
        w_high = sb("w_high", [P, len(SPLIT), GT, O], F32R)
        w_low = sb("w_low", [P, len(SPLIT), GT, O], F32R)
        cb_sb = sb("cb_sb", [P, 3])
        kept = sb("kept", [P, 2, C])
        feat = sb("feat", [P, 2, B])
        top3_sb = sb("top3_sb", [P, N2 // P])
        b2_sb = sb("b2_sb", [P, N2 // P])

        before_x = x_rot[:, 2, PART_0:, :].rearrange("p t n -> p (t n)")
        w0t_sb = before_x[:, 0:T0 * O].rearrange("p (t o) -> p t o", o=O)
        w_stage = before_x[:, T0 * O:T0 * O + len(SPLIT) * GT * O]
        after_x = x_rot[:, MLP_AFTER % SLOTS, :, :].rearrange("p t n -> p (t n)")
        parts = {}
        for name, size in (("top1", 2 * N1), ("top1d", N1), ("top2", N1 // P * N2), ("dense", B),
                           ("hid1", N1 // P * LOTS[0][1]), ("hid2", N2 // P * LOTS[0][1]), ("y", B)):
            parts[name], after_x = after_x[:, 0:size], after_x[:, size:]
        top1_sb = parts["top1"].rearrange("p (k n) -> p k n", n=N1)
        top1d_sb = parts["top1d"][0:D + 1, :]
        top2_sb = parts["top2"].rearrange("p (k n) -> p k n", n=N2)
        dense_sb = parts["dense"][0:D + 1, :]
        hid1 = parts["hid1"].rearrange("p (n b) -> p n b", b=LOTS[0][1])
        hid2 = parts["hid2"].rearrange("p (n b) -> p n b", b=LOTS[0][1])
        y_sb = parts["y"][0:1, :]

        side = ctx.enter_context(nc.psum_tensor("side", [P, N1 // P, 512], F32))
        y = [side[:, 0, :], side[:, 1, :], ps("y2")]
        x_near = side[:, 2, :]
        h = [side[:, 3, :], ps("h1")]
        rough_d = ctx.enter_context(nc.psum_tensor("rough_d", [P, GT, C], F32))
        m = [x_near, y[0]]

        s_ids = sem("s_ids")
        s_rows = sem("s_rows")
        s_gather = [sem(f"s_gather{k}") for k in range(SLOTS)]
        s_store = sem("s_store")
        s_store3 = sem("s_store3")
        s_start = [sem("s_start0"), sem("s_start1")]
        s_x = [[sem(f"s_x{a}{b}") for b in range(2)] for a in range(SLOTS)]
        s_w0 = sem("s_w0")
        s_w0ready = sem("s_w0ready")
        s_wp = sem("s_wp")
        s_stage = sem("s_stage")
        s_whigh = sem("s_whigh")
        s_wlow = sem("s_wlow")
        s_cb = sem("s_cb")
        s_top = sem("s_top")
        s_made0 = sem("s_made0")
        s_made = [sem("s_made1"), sem("s_made2")]
        s_high = [sem("s_high1"), sem("s_high2")]
        s_low = {kind: [sem(f"s_low{kind}{n}") for n in (1, 2)] for kind in "SD"}
        s_used = {-1: sem("s_used0"), 0: sem("s_used1"), 1: sem("s_used2")}
        s_near = sem("s_near")
        s_h = [sem("s_h0"), sem("s_h1")]
        s_kept = [sem(f"s_kept{k}") for k in range(3)]
        s_feat = [sem("s_feat01"), sem("s_feat2")]
        s_m1 = sem("s_m1")
        s_hid1 = sem("s_hid1")
        s_m2 = sem("s_m2")
        s_hid2 = sem("s_hid2")
        s_hid2b = sem("s_hid2b")
        s_m3 = sem("s_m3")
        s_ysb = sem("s_ysb")
        s_out = sem("s_out")

        block = ctx.enter_context(nc.Block())

        def over_steps(eng, step):
            for s in range(2):
                step(s, 0, s, s)
            with eng.Fori(0, (STEPS - 5) // SLOTS) as j:
                for s in range(2, 2 + SLOTS):
                    step(j * SLOTS + s, j + s // SLOTS, s % SLOTS, None)
            for s in range(STEPS - 3, STEPS):
                step(s, s // SLOTS, s % SLOTS, s)

        def bank(layer, first):
            return y[2] if layer == 1 and first else y[layer]

        KEEP = [slice(0, G), slice(G, P), slice(0, P)]
        HAND = [slice(G, P), slice(0, G)]
        SHIFT16 = slice(F * QD, F * QD + F)

        def loads(i, k):
            return 16 * ((Q + 1) * (i + 1) - (k == 0))

        def stored(c):
            return 16 * (REPS * (c + 1) - 1)

        def still(c):
            v = scratch[c, 0:F, :]
            return bass.AP(v.tensor, v.offset, [[0, Q], [C, F], [1, C]])

        def windows(c, row, tiles):
            v = scratch[c, row:row + F, :]
            return bass.AP(v.tensor, v.offset, [[C, F], [2 * C, tiles], [1, C]])

        @block.sync
        def _(sp):
            sp.dma_start(ids_sb[:, :], ids).then_inc(s_ids, 16)
            sp.dma_start(w0_sb[:, :, :], w0a).then_inc(s_w0, 16)
            sp.dma_start(w0t_sb[:, :, :], w0b).then_inc(s_w0, 16)
            sp.dma_start(w0d_sb[SHIFT16, :], w0d).then_inc(s_w0, 16)
            sp.dma_start(cb_sb[:, :], cin_bias).then_inc(s_cb, 16)
            sp.dma_start(w_stage, w_split).then_inc(s_stage, 16)
            sp.dma_start(wp_sb[:, :, :, :], w_plain).then_inc(s_wp, 16)

            def store(c, k, reps=range(REPS), done=s_store):
                for rep in reps:
                    sp.dma_start(scratch[c, F * rep:F * rep + F, :].rearrange("r (q n) -> q r n", q=Q),
                                 emb[:, k, :, :].rearrange("p j e -> p (j e)")).then_inc(done, 16)

            def store_all(c, i, k):
                sp.wait_ge(s_gather[k], 16 * JC * (i + 1))
                store(c, k)
                sp.wait_ge(s_store, stored(c))

            def load(c, k, t0, t1, done):
                for q in range(Q):
                    sp.dma_start(x_rot[F * q:F * q + F, k, t0:t1, :],
                                 windows(c, S0[q] + 2 * t0, t1 - t0)).then_inc(done, 16)

            def fetch(c, i, k, part, prior):
                t0, t1 = ((0, PART), (PART, T))[part]
                if part == 0:
                    sp.dma_start(x_still[:, :], still(c)).then_inc(s_x[k][0], 16)
                if prior:
                    sp.wait_ge(s_made[1], made(c - SLOTS, 1, t1 // GT - 1))
                load(c, k, t0, t1, s_x[k][part])

            sp.wait_ge(s_gather[0], 16 * JC)
            store(0, 0, range(2))
            sp.wait_ge(s_store, stored(0))
            sp.dma_start(x_still[:, :], still(0)).then_inc(s_start[0], 16)
            load(0, 0, 0, GT, s_start[0])
            load(0, 0, GT, T0 + 1, s_start[1])
            load(0, 0, T0 + 1, PART_0, s_x[0][0])
            store(0, 0, range(2, REPS), s_store3)
            sp.wait_ge(s_gather[1], 16 * JC)
            store(1, 1)
            sp.wait_ge(s_store3, 16)
            load(0, 0, PART_0, T, s_x[0][1])
            sp.wait_ge(s_store, stored(1))
            sp.wait_ge(s_used[-1], NG0)
            fetch(1, 0, 1, 0, False)
            fetch(1, 0, 1, 1, False)
            store_all(2, 0, 2)
            sp.wait_ge(s_used[-1], NG0 * 2)
            fetch(2, 0, 2, 0, False)
            sp.wait_ge(s_wlow, 1)
            fetch(2, 0, 2, 1, False)
            with sp.Fori(1, CHUNKS // SLOTS) as i:
                for k in range(SLOTS):
                    sp.wait_ge(s_used[-1], NG0 * (i * SLOTS + k))
                    store_all(i * SLOTS + k, i, k)
                    fetch(i * SLOTS + k, i, k, 0, True)
                    fetch(i * SLOTS + k, i, k, 1, True)
            for c in range(CHUNKS // SLOTS * SLOTS, CHUNKS):
                sp.wait_ge(s_used[-1], NG0 * c)
                store_all(c, c // SLOTS, c % SLOTS)
                fetch(c, c // SLOTS, c % SLOTS, 0, True)
                fetch(c, c // SLOTS, c % SLOTS, 1, True)
            sp.wait_ge(s_made[1], NG * (MLP_AFTER + 1))
            for dst, src in ((top1_sb, top1.rearrange("(k p) n -> p k n", p=P)), (top1d_sb, top1d),
                             (top2_sb, top2.rearrange("(k p) n -> p k n", p=P)),
                             (top3_sb[:, :], top3), (b2_sb[:, :], bias2), (dense_sb, dense)):
                sp.dma_start(dst, src).then_inc(s_top, 16)
            sp.wait_ge(s_ysb, len(LOTS))
            sp.dma_start(out, y_sb).then_inc(s_out, 16)
            sp.wait_ge(s_out, 16)

        @block.gpsimd
        def _(pool):
            def number_rows(c, k, prior=True):
                if prior:
                    pool.wait_ge(s_store, stored(c - SLOTS))
                nc.gpsimd.tensor_tensor(rows_sb[:, k, :], ids_sb[:, bass.ds(c * JC, JC)], base_sb,
                                        ALU.add).then_inc(s_rows, 1)

            def look_up(k):
                for j in range(JC):
                    nc.gpsimd.indirect_dma_start(
                        out=emb[:, k, j, :], out_offset=None, in_=tables,
                        in_offset=bass.IndirectOffsetOnAxis(ap=rows_sb[:, k, j:j + 1], axis=0),
                    ).then_inc(s_gather[k], 16)

            def take_low(c, layer, g):
                at = slot("parts S", layer, g)
                pool.wait_ge(s_high[layer], high_done(c, layer, g))
                nc.gpsimd.tensor_tensor(low["S"][:, at, :, :], rough[:, slot("rough S", layer, g), :, :],
                                        high["S"][:, at, :, :].bitcast(F32), ALU.subtract).then_inc(s_low["S"][layer], 1)

            def step(s, i, k, edge):
                ahead = 3 if edge == 0 else 2 if edge is None else 0
                k2 = (k + ahead) % SLOTS
                if edge == 0:
                    pool.wait_ge(s_store3, 16)
                if ahead:
                    number_rows(s + ahead, k2)
                if edge != LAST_STEP:
                    s_groups = [g for l, g in OF["S"] if l == 0]
                    for g in s_groups:
                        if ahead and g == s_groups[-1]:
                            pool.wait_ge(s_rows, s + ahead + 1)
                        take_low(s, 0, g)
                if ahead:
                    look_up(k2)
                if edge != 0:
                    for g in [g for l, g in OF["S"] if l == 1]:
                        take_low(s - 1, 1, g)

            pool.wait_ge(s_ids, 16)
            for c in range(SLOTS):
                number_rows(c, c, False)
                pool.wait_ge(s_rows, c + 1)
                look_up(c)
            assert STEPS - 4 + 2 == CHUNKS - 1
            over_steps(pool, step)

        @block.vector
        def _(dve):
            dve.wait_ge(s_w0, 48)
            for part, tiles in ((slice(F, G), slice(0, 1)), (slice(G, P), slice(0, 1)), (slice(0, P), slice(1, T0))):
                nc.vector.tensor_tensor(w0_sb[part, tiles, :], w0_sb[part, tiles, :], w0t_sb[part, tiles, :],
                                        ALU.add).then_inc(s_w0ready, 1)
            dve.wait_ge(s_whigh, 1)
            nc.vector.tensor_tensor(w_low[:, :, :, :].rearrange("p k t o -> p (k t o)"), w_stage,
                                    w_high[:, :, :, :].rearrange("p k t o -> p (k t o)").bitcast(F32),
                                    ALU.subtract).then_inc(s_wlow, 1)

            def twice(v):
                return v.rearrange("p (a n) -> p a n", a=1).to_broadcast([P, GT, C])

            def layer0(c, k, edge):
                first = edge == -1
                near = x_still[:, :] if first else x_near[:, :]
                if not first:
                    dve.wait_ge(s_near, c)
                for g in range(NG0 - 1):
                    if first:
                        dve.wait_ge(s_start[g], 16 * (Q if g else Q + 1))
                    last = last_user("P", c - 1, edge, -1, g)
                    if last:
                        dve.wait_ge(s_used[last[1]], used(*last))
                    nc.vector.tensor_tensor(prod[:, slot("P", -1, g), :, :], x_rot[:, k, GT * g:GT * g + GT, :],
                                            twice(near), ALU.mult).then_inc(s_made0, 1)
                if first:
                    dve.wait_ge(s_made0, NG0 - 1)
                nc.vector.tensor_tensor(x_still[SHIFT16, :], x_rot[SHIFT16, k, TD, :], near[SHIFT16, :],
                                        ALU.mult).then_inc(s_made0, 1)

            def make(s, k, edge, layer, g):
                kind = kind_of(layer, g)
                buf = {"P": "P", "S": "rough S", "D": "rough D"}[kind]
                dst = {"P": prod, "S": rough}[kind][:, slot(buf, layer, g), :, :] if kind != "D" else rough_d[:, :, :]
                last = last_user(buf, s, edge, layer, g)
                if last and kind == "P":
                    dve.wait_ge(s_used[last[1]], used(*last))
                elif last:
                    dve.wait_ge(s_low[kind][last[1]], low_done(*last))
                nc.vector.tensor_tensor(dst, x_rot[:, (k - layer) % SLOTS, GT * g:GT * g + GT, :],
                                        twice(h[layer][:, :]), ALU.mult).then_inc(s_made[layer], 1)

            def take_low(c, layer, g):
                at = slot("parts D", layer, g)
                dve.wait_ge(s_high[layer], high_done(c, layer, g))
                nc.vector.tensor_tensor(low["D"][:, at, :, :], rough_d[:, :, :],
                                        high["D"][:, at, :, :].bitcast(F32), ALU.subtract).then_inc(s_low["D"][layer], 1)

            def sum_lanes(c, n):
                dve.wait_ge(s_kept[n + 1], c + 1)
                nc.vector.tensor_reduce(feat[:, n, bass.ds(c * BC, BC)],
                                        kept[:, n, :].rearrange("p (b e) -> p b e", e=E),
                                        AX.X, ALU.add).then_inc(s_feat[n], 1)

            def scores(lot):
                a, b = LOTS[lot]
                dve.wait_ge(s_m3, lot + 1)
                nc.vector.tensor_copy(y_sb[:, a:b], m[0][0:1, 0:b - a]).then_inc(s_ysb, 1)

            def step(s, i, k, edge):
                if edge != LAST_STEP:
                    dve.wait_ge(s_h[0], 2 * (s + 1))
                    if edge == 0:
                        dve.wait_ge(s_x[0][0], loads(0, 0))
                    for g in range(NG):
                        if g == (PART_0 if edge == 0 else PART) // GT:
                            dve.wait_ge(s_x[k][1], 16 * Q * (i + 1))
                        make(s, k, edge, 0, g)
                        if g and kind_of(0, g - 1) == "D":
                            take_low(s, 0, g - 1)
                        if g == SUM_FIRST_AFTER and edge == 1:
                            sum_lanes(0, 0)
                        if g == SUM2_AFTER and edge not in (0, 1):
                            sum_lanes(s - 2, 1)
                if edge is None or s + 1 < CHUNKS:
                    layer0(s + 1, (k + 1) % SLOTS, edge)
                if edge == 0:
                    return
                dve.wait_ge(s_h[1], 2 * s)
                for g in range(NG):
                    make(s, k, edge, 1, g)
                    if g and kind_of(1, g - 1) == "D":
                        take_low(s - 1, 1, g - 1)
                    if g == SUM1_AFTER:
                        if edge != LAST_STEP:
                            sum_lanes(s, 0)
                        else:
                            sum_lanes(s - 2, 1)
                if edge == LAST_STEP:
                    scores(0)
                    sum_lanes(s - 1, 1)

            SUM2_AFTER, SUM1_AFTER = 6, 2
            SUM_FIRST_AFTER = 5
            assert KINDS[0][-1] != "D" and KINDS[1][-1] != "D"
            layer0(0, 0, -1)
            over_steps(dve, step)
            dve.wait_ge(s_m2, 2 * (N2 // P))
            nc.vector.tensor_scalar(hid2[:, 1, 0:LAST], m[1][:, 0:LAST], b2_sb[:, 1:2], 0.0,
                                    ALU.add, ALU.max).then_inc(s_hid2b, 1)
            scores(1)

        @block.scalar
        def _(act):
            act.wait_ge(s_stage, 16)
            nc.scalar.activation(w_high[:, :, :, :].rearrange("p k t o -> p (k t o)"), w_stage,
                                 ACT.Copy).then_inc(s_whigh, 1)
            act.wait_ge(s_cb, 16)

            def relu(dst, layer, part, first):
                return nc.scalar.activation(dst, bank(layer, first)[part, :], ACT.Relu, bias=cb_sb[part, layer:layer + 1])

            def hand_on(c, layer, first):
                if not first:
                    act.wait_ge(s_made[layer], NG * c)
                relu(h[layer][0:G, :], layer, HAND[layer], first).then_inc(s_h[layer], 1)
                relu(h[layer][G:P, :], layer, HAND[layer], first).then_inc(s_h[layer], 1)

            def keep(c, layer, first):
                if not first:
                    act.wait_ge(s_feat[layer // 2], c)
                relu(kept[KEEP[layer], layer // 2, :], layer, KEEP[layer], first).then_inc(s_kept[layer], 1)

            def layer0(c, first):
                act.wait_ge(s_used[-1], NG0 * (c + 1))
                hand_on(c, 0, first)

            def round_high(s, edge, layer, g):
                kind = kind_of(layer, g)
                last = last_user(f"parts {kind}", s, edge, layer, g)
                if last:
                    act.wait_ge(s_used[last[1]], used(*last))
                act.wait_ge(s_made[layer], made(s - layer, layer, g))
                src = rough[:, slot("rough S", layer, g), :, :] if kind == "S" else rough_d[:, :, :]
                nc.scalar.activation(high[kind][:, slot(f"parts {kind}", layer, g), :, :], src,
                                     ACT.Copy).then_inc(s_high[layer], 1)

            def bring_near(c, i, k):
                act.wait_ge(s_x[k][0], loads(i, k))
                act.wait_ge(s_made0, NG0 * c)
                nc.scalar.activation(x_near[:, :], x_still[:, :], ACT.Copy).then_inc(s_near, 1)

            def hidden1(n):
                act.wait_ge(s_m1, n + 1)
                nc.scalar.activation(hid1[:, n, :], m[n % 2][:, 0:LOTS[0][1]], ACT.Relu).then_inc(s_hid1, 1)

            def hidden2(lot, n):
                a, b = LOTS[lot]
                act.wait_ge(s_m2, N2 // P * lot + n + 1)
                nc.scalar.activation(hid2[:, n, 0:b - a], m[n][:, 0:b - a], ACT.Relu,
                                     bias=b2_sb[:, n:n + 1]).then_inc(s_hid2, 1)

            def step(s, i, k, edge):
                split1 = [g for l, g in SPLIT if l == 0]
                split2 = [g for l, g in SPLIT if l == 1]
                if edge != LAST_STEP:
                    groups = split1[0 if edge in (0, 1) else EARLY:]
                    for n, g in enumerate(groups):
                        if edge == 1 and n == TAKE_FIRST_AT:
                            act.wait_ge(s_used[0], NG)
                            hand_on(0, 1, True)
                            keep(0, 1, True)
                        round_high(s, edge, 0, g)
                        if n == (len(groups) - 1 if edge == 0 else NEAR_AFTER) and (edge is None or s + 1 < CHUNKS):
                            bring_near(s + 1, i + (k + 1) // SLOTS, (k + 1) % SLOTS)
                        if edge == 1 and n == TAKE_FIRST_AT:
                            keep(1, 0, False)
                if edge == 0:
                    layer0(1, False)
                    return
                for n, g in enumerate(split2):
                    if n == KEEP1_AFTER and edge != LAST_STEP:
                        act.wait_ge(s_used[0], NG * (s + 1))
                        keep(s, 1, False)
                        if edge == LAST_STEP - 1:
                            act.wait_ge(s_top, 16 * 6)
                            hidden1(0)
                            hidden1(1)
                    if n == LAYER0_AFTER and (edge is None or s + 1 < CHUNKS):
                        layer0(s + 1, False)
                        keep(s + 1, 0, False)
                    round_high(s, edge, 1, g)
                    if edge == LAST_STEP - 1 and KEEP1_AFTER <= n < KEEP1_AFTER + 2:
                        hidden1(n - KEEP1_AFTER + 2)
                    if edge == LAST_STEP and n < N2 // P:
                        hidden2(0, n)
                if edge != LAST_STEP:
                    hand_on(s, 1, False)
                    if edge != LAST_STEP - 1:
                        for g in split1[:EARLY]:
                            round_high(s + 1, None if edge is None else edge + 1, 0, g)
                act.wait_ge(s_used[1], NG * s)
                keep(s - 1, 2, edge == 1)

            TAKE_FIRST_AT = 3
            NEAR_AFTER = 2
            KEEP1_AFTER = 0
            LAYER0_AFTER = 3
            layer0(0, True)
            keep(0, 0, True)
            over_steps(act, step)
            act.wait_ge(s_m1, N1 // P + 1)
            nc.scalar.activation(hid1[:, :, 0:LAST], side[:, :, 0:LAST], ACT.Relu).then_inc(s_hid1, 1)
            hidden2(1, 0)

        @block.tensor
        def _(pe):
            def layer0(c, first):
                if not first:
                    pe.wait_ge(s_kept[0], c)
                for g in range(NG0 - 1):
                    pe.wait_ge(s_made0, NG0 * c + g + 1)
                    for t in range(GT):
                        mm = nc.tensor.matmul(y[0][:, :], w0_sb[:, GT * g + t, :], prod[:, slot("P", -1, g), t, :],
                                              start=g == 0 and t == 0, stop=False)
                    mm.then_inc(s_used[-1], 1)
                pe.wait_ge(s_made0, NG0 * (c + 1))
                nc.tensor.matmul(y[0][:, :], w0d_sb[SHIFT16, :], x_still[SHIFT16, :],
                                 start=False, stop=True).then_inc(s_used[-1], 1)

            def layer(s, l, edge, between=None, at_group=None):
                c = s - l
                total = bank(l + 1, edge == 0)[:, :]
                if edge == l == 1:
                    pe.wait_ge(s_kept[1], 1)
                elif edge not in (0, 1):
                    pe.wait_ge(s_kept[l + 1], c)
                    if l == 0:
                        pe.wait_ge(s_h[1], 2 * c)
                for n, g in enumerate(USE[l]):
                    if n == at_group:
                        between()
                    start, stop = n == 0, n == NG - 1
                    kind = kind_of(l, g)
                    if kind == "P":
                        pe.wait_ge(s_made[l], made(c, l, g))
                        for t in range(GT):
                            mm = nc.tensor.matmul(total, wp_sb[:, OF["P"].index((l, g)), t, :],
                                                  prod[:, slot("P", l, g), t, :],
                                                  start=start and t == 0, stop=stop and t == GT - 1)
                    else:
                        k, at = SPLIT.index((l, g)), slot(f"parts {kind}", l, g)
                        pe.wait_ge(s_low[kind][l], low_done(c, l, g))
                        for t in range(GT):
                            w_hi, w_lo = w_high[:, k, t, :], w_low[:, k, t, :]
                            hi, lo = high[kind][:, at, t, :], low[kind][:, at, t, :]
                            nc.tensor.matmul(total, w_hi, hi, start=start and t == 0, stop=False)
                            nc.tensor.matmul(total, w_hi, lo, start=False, stop=False)
                            mm = nc.tensor.matmul(total, w_lo, hi, start=False, stop=stop and t == GT - 1)
                    mm.then_inc(s_used[l], 1)

            WARM_BEFORE, WARM_BETWEEN, WARM_LAST = 4, 4, 1

            def keep_warm(n, unused):
                for _ in range(n):
                    nc.tensor.matmul(unused, w0_sb[:, 0, :], wp_sb[:, 0:2, :, :].rearrange("p k t o -> p (k t o)"),
                                     start=True, stop=True)

            def mlp1_first():
                rows = slice(*LOTS[0])
                pe.wait_ge(s_made0, NG0 * CHUNKS)
                pe.wait_ge(s_kept[0], CHUNKS)
                for k in range(2):
                    pe.wait_ge(s_feat[k], LOTS[0][1] // BC)
                for n in range(N1 // P):
                    if n >= 2:
                        pe.wait_ge(s_hid1, n - 1)
                    cols, total = slice(P * n, P * n + P), m[n % 2][:, rows]
                    nc.tensor.matmul(total, top1_sb[:, 0, cols], feat[:, 0, rows], start=True, stop=False)
                    nc.tensor.matmul(total, top1_sb[:, 1, cols], feat[:, 1, rows], start=False, stop=False)
                    nc.tensor.matmul(total, top1d_sb[:, cols], dense_sb[:, rows],
                                     start=False, stop=True).then_inc(s_m1, 1)

            def mlp1_last():
                rows = slice(*LOTS[1])
                pe.wait_ge(s_hid2, N2 // P)
                pe.wait_ge(s_ysb, 1)
                pe.wait_ge(s_made[0], NG * CHUNKS)
                pe.wait_ge(s_feat[0], CHUNKS)
                for n in range(N1 // P):
                    cols, total = slice(P * n, P * n + P), side[:, n, 0:LAST]
                    nc.tensor.matmul(total, top1_sb[:, 0, cols], feat[:, 0, rows], start=True, stop=False)
                    nc.tensor.matmul(total, top1d_sb[:, cols], dense_sb[:, rows], start=False, stop=False)
                keep_warm(WARM_LAST, rough_d[:, 0, :])
                pe.wait_ge(s_feat[1], CHUNKS)
                for n in range(N1 // P):
                    cols, total = slice(P * n, P * n + P), side[:, n, 0:LAST]
                    mm = nc.tensor.matmul(total, top1_sb[:, 1, cols], feat[:, 1, rows], start=False, stop=True)
                mm.then_inc(s_m1, 1)

            def mlp2(lot):
                a, b = LOTS[lot]
                for n in range(N2 // P):
                    for k in range(N1 // P):
                        if n == 0 or not lot:
                            pe.wait_ge(s_hid1, N1 // P + 1 if lot else k + 1 if n else N1 // P)
                        mm = nc.tensor.matmul(m[n][:, 0:b - a], top2_sb[:, k, P * n:P * n + P],
                                              hid1[:, k, 0:b - a], start=k == 0, stop=k == N1 // P - 1)
                    mm.then_inc(s_m2, 1)

            def mlp3(lot):
                a, b = LOTS[lot]
                pe.wait_ge(s_hid2, N2 // P + lot)
                if lot:
                    pe.wait_ge(s_hid2b, 1)
                for k in range(N2 // P):
                    mm = nc.tensor.matmul(m[0][0:1, 0:b - a], top3_sb[:, k:k + 1], hid2[:, k, 0:b - a],
                                          start=k == 0, stop=k == N2 // P - 1)
                mm.then_inc(s_m3, 1)

            def step(s, i, k, edge):
                if edge == 0:
                    layer(0, 0, 0, lambda: layer0(1, False), L0_WITHIN)
                elif edge != LAST_STEP:
                    layer(s, 0, edge)
                if edge is None or 0 < s < CHUNKS - 1:
                    layer0(s + 1, False)
                if edge == LAST_STEP - 1:
                    pe.wait_ge(s_top, 16 * 6)
                    mlp1_first()
                if edge == LAST_STEP:
                    mlp2(0)
                if edge != 0:
                    layer(s, 1, edge, lambda: mlp3(0), NG // 2 if edge == LAST_STEP else None)

            L0_WITHIN = 5
            pe.wait_ge(s_w0ready, 3)
            pe.wait_ge(s_wp, 16)
            pe.wait_ge(s_store, 16 * 2)
            keep_warm(WARM_BEFORE, y[1])
            layer0(0, True)
            keep_warm(WARM_BETWEEN, y[1])
            pe.wait_ge(s_wlow, 1)
            over_steps(pe, step)
            mlp1_last()
            mlp2(1)
            mlp3(1)


def kernel(**inputs):
    import concourse.bacc as bacc
    from concourse.bass_utils import run_bass_kernel_spmd

    a = {k: np.asarray(v) for k, v in inputs.items()}
    tables = [a[f"tbl_{f}"] for f in range(F)]
    first_row = np.cumsum([0] + [t.shape[0] for t in tables[:-1]]).astype(np.int32)

    p = np.arange(P)
    shift = np.array(S0)[p // F][:, None] + 2 * np.arange(T)[None, :]
    f12 = (shift + (p % F)[:, None]) % F
    pair12 = f12 * G + (p % G)[:, None]
    r0 = (p % F)[:, None] + 0 * f12[:, :T0]
    w0 = a["L0_rec_W0"].T
    w1 = np.roll(a["L0_rec_W1"], G, axis=0).T
    b1 = np.roll(a["L0_rec_b1"], G)
    w12 = np.stack([w1[pair12], a["L0_rec_W2"].T[pair12]], axis=1).reshape(P, 2, NG, GT, O)
    arrays = {
        "ids": np.concatenate([a["ids"].reshape(CHUNKS, Q, JC, F).transpose(1, 3, 0, 2).reshape(P, B // Q),
                               np.repeat(np.tile(first_row, Q)[:, None], JC, axis=1)], axis=1),
        "tables": np.concatenate(tables, axis=0),
        "dense": np.concatenate([a["dense_ctx"].T, np.ones((1, B), np.float32)]),
        "w0a": w0[r0 * F + f12[:, :T0]],
        "w0b": w0[f12[:, :T0] * F + r0],
        "w0d": w0[np.arange(F) * F + (np.arange(F) + F // 2) % F],
        "w_plain": np.stack([w12[:, layer, g] for layer, g in OF["P"]], axis=1),
        "w_split": np.stack([w12[:, layer, g] for layer, g in SPLIT], axis=1).reshape(P, -1),
        "cin_bias": np.stack([a["L0_rec_b0"], b1, a["L0_rec_b2"]], axis=1),
        "top1": a["W_top1"][:2 * P],
        "top1d": np.concatenate([a["W_top1"][2 * P:], a["b_top1"][None]]),
        "top2": a["W_top2"],
        "bias2": a["b_top2"].reshape(N2 // P, P).T,
        "top3": a["W_top3"].reshape(N2 // P, P).T,
    }
    nc = bacc.Bacc("TRN2", target_bir_lowering=False, num_devices=1)
    feeds, args = {}, []
    for name, v in arrays.items():
        v = np.ascontiguousarray(v)
        feeds[f"in_{name}"] = v
        args.append(nc.dram_tensor(f"in_{name}", v.shape, mybir.dt.from_np(v.dtype), kind="ExternalInput").ap())
    args.append(nc.dram_tensor("scratch", (CHUNKS, REPS * F, C), F32, kind="Internal").ap())
    args.append(nc.dram_tensor("out_y", (1, B), F32, kind="ExternalOutput").ap())
    dlrm_tower(nc, *args)
    r = run_bass_kernel_spmd(nc, [feeds], core_ids=[0])
    return r.results[0]["out_y"].reshape(B, 1)
```
